# Optimizing a Trainium2 kernel written in Bass

```python
import numpy as np
import jax
import jax.numpy as jnp

def _softmax(x, axis=-1):
    return jax.nn.softmax(x, axis=axis)

def _gelu(x):
    return jax.nn.gelu(x, approximate=True)

def _silu(x):
    return jax.nn.silu(x)

def _sigmoid(x):
    return jax.nn.sigmoid(x)

def _layernorm(x, axis=-1, eps=1e-05):
    m = jnp.mean(x, axis=axis, keepdims=True)
    v = jnp.var(x, axis=axis, keepdims=True)
    return (x - m) / jnp.sqrt(v + eps)

def _scatter_add(tgt, idx, src, axis=0):
    return tgt.at[idx].add(src)

def _segment_sum(src, seg, n):
    return jax.ops.segment_sum(src, seg, n)
kernel_name = 'mk_xattn_seq_d1_seqx_r4_e1c75d'

def setup_inputs(seed: int=0):
    np.random.seed(seed)
    _w = jnp.asarray

    def _rec_inputs():
        import jax
        import jax.numpy as jnp
        _rk = jax.random.key(seed)
        x = -0.0002928 + 1 * jax.random.normal(jax.random.fold_in(_rk, 1), (128, 128, 256), jnp.float32)
        _lenS = 128 - jax.random.randint(jax.random.fold_in(_rk, 7), (128,), 0, max(1, 128 // 4) + 1, jnp.int32)
        _lenS2 = 128 - jax.random.randint(jax.random.fold_in(_rk, 8), (128,), 0, max(1, 128 // 4) + 1, jnp.int32)
        _ctx_1024P = jax.random.normal(jax.random.fold_in(_rk, 11), (128, 16, 256), jnp.float32)
        _ctx_1024c = jax.random.dirichlet(jax.random.fold_in(_rk, 511), 0.3 * jnp.ones((16,), jnp.float32), (128, 128))
        _ctx_1024t = jnp.einsum('bsk,bkd->bsd', _ctx_1024c, _ctx_1024P)
        _ctx_1024t = _ctx_1024t * jax.lax.rsqrt(jnp.mean(jnp.square(_ctx_1024t)) + 1e-12) * 0.953939
        ctx_1024 = -1.39393e-06 + 0.999914 * (_ctx_1024t + 0.3 * jax.random.normal(jax.random.fold_in(_rk, 611), (128, 128, 256), jnp.float32))
        return (x, ctx_1024)
    x, ctx_1024 = _rec_inputs()

    def _L0_xattn_setup():
        import jax, jax.numpy as jnp
        import numpy as np
        B, S, H, N_HEAD = (2, 512, 256, 16)
        NEG = float(-2 ** 32 + 1)
        EPS = 1e-08
        key = jax.random.key(seed)
        ks = jax.random.split(key, 11)
        sc = 0.02
        return {'queries': jax.random.normal(ks[0], (B, S, H), dtype=jnp.float32), 'keys': jax.random.normal(ks[1], (B, S, H), dtype=jnp.float32), 'values': jax.random.normal(ks[2], (B, S, H), dtype=jnp.float32), 'Wq': jax.random.normal(ks[3], (H, H), dtype=jnp.float32) * sc, 'bq': jax.random.normal(ks[4], (H,), dtype=jnp.float32) * sc, 'Wk': jax.random.normal(ks[5], (H, H), dtype=jnp.float32) * sc, 'bk': jax.random.normal(ks[6], (H,), dtype=jnp.float32) * sc, 'Wv': jax.random.normal(ks[7], (H, H), dtype=jnp.float32) * sc, 'bv': jax.random.normal(ks[8], (H,), dtype=jnp.float32) * sc, 'Wo': jax.random.normal(ks[9], (H, H), dtype=jnp.float32) * sc, 'bo': jax.random.normal(ks[10], (H,), dtype=jnp.float32) * sc}
    _L0_xattn_all = _L0_xattn_setup()
    _L0_xattn_in = {k: v for k, v in _L0_xattn_all.items() if k in ('Wq', 'bq', 'Wk', 'bk', 'Wv', 'bv', 'Wo', 'bo')}
    del _L0_xattn_all
    return {'x': x, 'ctx_1024': ctx_1024, 'L0_xattn_Wq': _L0_xattn_in['Wq'], 'L0_xattn_bq': _L0_xattn_in['bq'], 'L0_xattn_Wk': _L0_xattn_in['Wk'], 'L0_xattn_bk': _L0_xattn_in['bk'], 'L0_xattn_Wv': _L0_xattn_in['Wv'], 'L0_xattn_bv': _L0_xattn_in['bv'], 'L0_xattn_Wo': _L0_xattn_in['Wo'], 'L0_xattn_bo': _L0_xattn_in['bo']}

def reference(x, ctx_1024, L0_xattn_Wq, L0_xattn_bq, L0_xattn_Wk, L0_xattn_bk, L0_xattn_Wv, L0_xattn_bv, L0_xattn_Wo, L0_xattn_bo):
    import jax
    import jax.numpy as jnp

    def _L0_xattn_ref(queries, keys, values, Wq, bq, Wk, bk, Wv, bv, Wo, bo):
        import jax, jax.numpy as jnp
        import numpy as np
        B, S, H, N_HEAD = (2, 512, 256, 16)
        NEG = float(-2 ** 32 + 1)
        EPS = 1e-08
        n = N_HEAD
        Bb, Sq, Hh = queries.shape
        Sk = keys.shape[1]
        d = Hh // n
        Q = jax.nn.relu(queries @ Wq + bq)
        K = jax.nn.relu(keys @ Wk + bk)
        V = jax.nn.relu(values @ Wv + bv)
        Q_ = Q.reshape(Bb, Sq, n, d).transpose(2, 0, 1, 3)
        K_ = K.reshape(Bb, Sk, n, d).transpose(2, 0, 1, 3)
        V_ = V.reshape(Bb, Sk, n, d).transpose(2, 0, 1, 3)
        key_masks = jnp.sign(jnp.abs(jnp.sum(K, axis=-1)))
        scores = jnp.einsum('hbqd,hbkd->hbqk', Q_, K_) / d ** 0.5
        scores = jnp.where(key_masks[None, :, None, :] == 0.0, NEG, scores)
        tril = jnp.tril(jnp.ones((Sq, Sk), dtype=scores.dtype))
        scores = jnp.where(tril[None, None] == 0.0, NEG, scores)
        attn = jax.nn.softmax(scores, axis=-1)
        out = jnp.einsum('hbqk,hbkd->hbqd', attn, V_)
        out = out.transpose(1, 2, 0, 3).reshape(Bb, Sq, Hh)
        out = jax.nn.relu(out @ Wo + bo)
        out = queries + out
        mean = out.mean(axis=-1, keepdims=True)
        std = jnp.std(out, axis=-1, ddof=1, keepdims=True)
        return (out - mean) / (std + EPS)
    x = _L0_xattn_ref(x, ctx_1024, ctx_1024, L0_xattn_Wq, L0_xattn_bq, L0_xattn_Wk, L0_xattn_bk, L0_xattn_Wv, L0_xattn_bv, L0_xattn_Wo, L0_xattn_bo)
    return x

_drawn_inputs = setup_inputs


def setup_inputs(seed=0):
    import zlib

    import numpy as np

    out = dict(_drawn_inputs(seed))
    spreads = {}
    factors = {'ctx_1024': 3.093,
     'L0_xattn_Wq': 8.0,
     'L0_xattn_bq': 8.0,
     'L0_xattn_Wk': 8.0,
     'L0_xattn_bk': 49.5,
     'L0_xattn_Wv': 3.049,
     'L0_xattn_bv': 21.733,
     'L0_xattn_bo': 4.191}
    for name, (base, spread) in spreads.items():
        noise = np.random.default_rng([zlib.crc32(name.encode()), seed]).standard_normal(out[name].shape)
        drawn = base * np.exp(spread * noise) if base else spread * noise
        out[name] = jnp.asarray(drawn.astype(out[name].dtype))
    for name, factor in factors.items():
        out[name] = (out[name] * factor).astype(out[name].dtype)
    return out
```

```python
from contextlib import ExitStack

import numpy as np
import concourse.bass as bass
import concourse.mybir as mybir
from concourse.alu_op_type import AluOpType as ALU

F32 = mybir.dt.float32
F32R = mybir.dt.float32r
BF16 = mybir.dt.bfloat16
ACT = mybir.ActivationFunctionType
AX = mybir.AxisListType

P = 128
NB = 128
H = 256
KT = H // P
NH = 16
D = H // NH
G = 4
NG = NB // G
GT = G * P
CH = 4
NC = NH // CH
HB = 8
SLOTS = 6
SHIFT_ROW = SLOTS * D
MASK_ROW = SHIFT_ROW + 2
MASK_W = 5
MASK_N = -(-P // MASK_W)
MASK_END = MASK_ROW + MASK_N
Q_PARTS = (0, 0, 0, 1, 1, 2)
K_PARTS = (0, 1, 2, 0, 1, 0)
EPS = 1e-8

LV = 2
LB = 6
LC = 8
LW = 14
RING = 8
SLOT_END = 152
LOOP_FROM, LOOP_TO = 24, 120


class Slot:

    def __init__(self, n, i=None):
        self.n, self.i = n, i

    def at(self, value, per_iteration):
        return value if self.i is None else value + per_iteration * self.i

    def chunks(self, value):
        return self.at(value, RING * NC)

    def seqs(self, value):
        return self.at(value, RING)

    def groups(self, value):
        return self.at(value, RING // G)

    def has(self, index, total):
        return 0 <= index < total


def wait(eng, sem, value, alone=False):
    if not isinstance(value, int) or value > 0:
        eng.wait_ge(sem, value)
        if alone and not isinstance(value, int):
            eng.nop(nofuse=True)


def run_slots(eng, body):
    for n in range(LOOP_FROM):
        body(Slot(n))
    with eng.Fori(0, (LOOP_TO - LOOP_FROM) // RING) as i:
        for k in range(RING):
            body(Slot(LOOP_FROM + k, i))
    for n in range(LOOP_TO, SLOT_END):
        body(Slot(n))


def build(nc, xT, cT, x, wq, wk, wv, wo, bqk, bvo, ident, mask_q, mask_k, out):
    xT_v = xT.rearrange("(k p) t -> p k t", p=P)
    cT_v = cT.rearrange("(k p) t -> p k t", p=P)
    x_v = x.rearrange("b q f -> q b f")
    out_v = out.rearrange("b q f -> q b f")
    recip_dram = nc.dram_tensor("recip_dram", (2, NH * GT), F32, kind="Internal").ap()

    with ExitStack() as ctx:
        def sb(name, shape, dt=F32):
            return ctx.enter_context(nc.sbuf_tensor(name, shape, dt))

        def sem(name):
            return ctx.enter_context(nc.semaphore(name))

        def bank(name):
            return ctx.enter_context(nc.psum_tensor(name, [P, 512], F32))

        w_hi = [sb(f"w_hi{j}", [P, KT, H], F32R) for j in range(4)]
        w_lo = [sb(f"w_lo{j}", [P, KT, H], F32R) for j in range(4)]
        bias_qk = sb("bias_qk", [P, 2, KT])
        bias_parts = sb("bias_parts", [3, 2 * H], BF16)
        id_f32 = sb("id_f32", [P, P])
        ones_bf = sb("ones_bf", [P, P], BF16)
        zeros_bf = sb("zeros_bf", [2, 2 * P], BF16)
        masks_bf = sb("masks_bf", [MASK_N, 2, P], BF16)
        half = sb("half", [P, G])
        id_bf = sb("id_bf", [P, P], BF16)
        causal = sb("causal", [P, P], BF16)
        xT_raw = sb("xT_raw", [P, KT, GT])
        cT_raw = sb("cT_raw", [P, KT, GT])
        xT_hi = sb("xT_hi", [P, KT, GT], F32R)
        xT_lo = sb("xT_lo", [P, KT, GT], F32R)
        cT_hi = [sb(f"cT_hi{j}", [P, KT, GT], F32R) for j in range(2)]
        cT_lo = [sb(f"cT_lo{j}", [P, KT, GT], F32R) for j in range(2)]
        x_rows = [sb(f"x_rows{j}", [P, G, H]) for j in range(2)]
        proj = sb("proj", [P, KT, GT])
        rest = sb("rest", [P, KT, GT])
        parts = [[sb(f"part{m}_{j}", [P, KT, GT], BF16) for m in range(3)] for j in range(2)]
        stack_q = [sb(f"stack_q{j}", [P, NH, GT], BF16) for j in range(2)]
        stack_k = [sb(f"stack_k{j}", [P, NH, GT], BF16) for j in range(2)]
        v_aug = sb("v_aug", [P, RING, NH, 2 * D])
        neg_max = sb("neg_max", [P, 2, NH])
        shift = sb("shift", [NH, 2, 2, P], BF16)
        key_bias = sb("key_bias", [P, RING])
        probs = sb("probs", [P, 4, CH * P])
        o_raw = [sb(f"o_raw{j}", [P, NC, GT]) for j in range(2)]
        den = sb("den", [P, 64])
        den_ok = sb("den_ok", [P, 64])
        recip = sb("recip", [P, 64])
        o_all = sb("o_all", [P, KT, GT])
        recip_all = sb("recip_all", [P, KT, GT])
        o_hi = sb("o_hi", [P, KT, GT], F32R)
        o_lo = sb("o_lo", [P, KT, GT], F32R)
        z = [sb(f"z{j}", [P, G, H]) for j in range(2)]
        bias_row = z[0][0:1, 0:2, :].rearrange("p a f -> p (a f)")
        bias_rest = z[0][0:1, 2:4, :].rearrange("p a f -> p (a f)")
        bias_parts1 = stack_q[0][0:1, 0:3, :]
        masks_f = z[1][0:MASK_N, 0, :].rearrange("p (a t) -> p a t", a=2)
        stats = sb("stats", [P, 6])
        mean_var = sb("mean_var", [P, 2, G, 2])
        var_n1 = sb("var_n1", [P, G])
        std = sb("std", [P, G])
        std_eps = sb("std_eps", [P, G])
        rstd = sb("rstd", [P, G])
        neg_mean_rstd = sb("neg_mean_rstd", [P, G])

        s_bank = [bank(f"s_bank{j}") for j in range(2)]
        st_bank = [bank(f"st_bank{j}") for j in range(2)]
        pv_bank = bank("pv_bank")
        qk_bank = bank("qk_bank")
        v_bank = bank("v_bank")
        misc_bank = bank("misc_bank")

        w_in = sem("w_in")
        const_in = sem("const_in")
        mask_in = sem("mask_in")
        bias_in = sem("bias_in")
        bias_parts_in = sem("bias_parts_in")
        xT_in = sem("xT_in")
        cT_in = sem("cT_in")
        rows_in = [sem(f"rows_in{j}") for j in range(2)]
        stack_in = [[sem(f"stack_in{j}_{h}") for h in range(2)] for j in range(2)]
        shift_in = [sem(f"shift_in{j}") for j in range(2)]
        den_in = sem("den_in")
        num_in = sem("num_in")
        recip_out = sem("recip_out")
        recip_in = sem("recip_in")
        stored = [sem(f"stored{j}") for j in range(2)]
        w_hi_done = sem("w_hi_done")
        w_lo_done = sem("w_lo_done")
        bias_step = sem("bias_step")
        masks_done = sem("masks_done")
        pool_const = sem("pool_const")
        qk_ready = sem("qk_ready")
        v_ready = sem("v_ready")
        s_ready = sem("s_ready")
        st_ready = sem("st_ready")
        pv_ready = sem("pv_ready")
        shiftT_ready = sem("shiftT_ready")
        ksum_ready = sem("ksum_ready")
        wo_ready = sem("wo_ready")
        qk_evac = sem("qk_evac")
        v_evac = sem("v_evac")
        exp_done = sem("exp_done")
        o_evac = sem("o_evac")
        x_hi_done = sem("x_hi_done")
        c_hi_done = sem("c_hi_done")
        o_hi_done = sem("o_hi_done")
        norm_done = sem("norm_done")
        max_done = sem("max_done")
        shift1_done = sem("shift1_done")
        shift_done = sem("shift_done")
        key_bias_done = sem("key_bias_done")
        part1_done = sem("part1_done")
        part2_done = sem("part2_done")
        x_lo_done = sem("x_lo_done")
        c_lo_done = sem("c_lo_done")
        o_lo_done = sem("o_lo_done")
        den_ok_done = sem("den_ok_done")
        recip_done = sem("recip_done")
        z_done = sem("z_done")
        stats_done = sem("stats_done")
        aggr_done = sem("aggr_done")
        var_done = sem("var_done")
        std_eps_done = sem("std_eps_done")
        rstd_done = sem("rstd_done")
        scale_done = sem("scale_done")
        rest_done = sem("rest_done")
        part3_done = sem("part3_done")
        mult_done = sem("mult_done")
        std_done = sem("std_done")

        block = ctx.enter_context(nc.Block())

        def tok(b):
            return slice((b % G) * P, (b % G) * P + P)

        @block.sync
        def _(sp):
            sp.dma_start(id_f32[:], ident).then_inc(const_in, 16)
            sp.dma_start(bias_qk[:], bqk).then_inc(const_in, 16)
            sp.dma_start(bias_row, bvo).then_inc(bias_in, 16)
            sp.dma_start(masks_f[:, 0, :], mask_q).then_inc(mask_in, 16)
            sp.dma_start(masks_f[:, 1, :], mask_k).then_inc(mask_in, 16)
            for j, (w, raw) in enumerate(zip((wq, wk, wv, wo), (proj, rest, o_all, recip_all))):
                sp.dma_start(raw[:, :, 0:H], w.rearrange("(k p) f -> p k f", p=P)).then_inc(w_in, 16)
            sp.wait_ge(bias_step, 4)
            sp.dma_start(bias_parts[:], bias_parts1.rearrange("a m f -> a (m f)")).then_inc(bias_parts_in, 16)
            sp.wait_ge(masks_done, 1)
            for j in range(2):
                for m, stack in enumerate((stack_q[j], stack_k[j])):
                    dst = stack[MASK_ROW:MASK_END, :, :].rearrange("p h (b t) -> p (h b) t", t=P)
                    src = masks_bf[:, m, :].unsqueeze(1).to_broadcast([MASK_N, NH * G, P])
                    sp.dma_start(dst, src).then_inc(const_in, 16)
            sp.wait_ge(pool_const, 1)
            for j in range(2):
                dst = stack_k[j][SHIFT_ROW:MASK_ROW, :, :].rearrange("p h (b t) -> p (h b) t", t=P)
                src = ones_bf[0:2, :].unsqueeze(1).to_broadcast([2, NH * G, P])
                sp.dma_start(dst, src).then_inc(const_in, 16)
            sp.dma_start(xT_raw[:], xT_v[:, :, 0:GT]).then_inc(xT_in, 16)
            sp.dma_start(cT_raw[:], cT_v[:, :, 0:GT]).then_inc(cT_in, 16)

            def fill_stack(s, g, tensor, halves):
                j = g % 2
                stack = (stack_q, stack_k)[tensor][j]
                order = (Q_PARTS, K_PARTS)[tensor]
                wait(sp, part3_done, s.at(2 * (2 * g + tensor + 1), 2 * 4), True)
                for half_ in halves:
                    cols = slice(half_ * 2 * P, (half_ + 1) * 2 * P)
                    wait(sp, st_ready, s.chunks(NC * (G * (g - 2) + 2 * half_ + 2)), True)
                    for slot in range(SLOTS):
                        for t in range(KT):
                            sp.dma_start(stack[D * slot:D * slot + D, HB * t:HB * t + HB, cols],
                                         parts[tensor][order[slot]][:, t, cols]).then_inc(stack_in[j][half_], 16)
                    if tensor == 0:
                        src = zeros_bf[:, :].unsqueeze(1).to_broadcast([2, NH, 2 * P])
                        sp.dma_start(stack[SHIFT_ROW:MASK_ROW, :, cols], src).then_inc(stack_in[j][half_], 16)

            def slot(s):
                n, r = s.n, s.n % G
                g = n // G + 1
                if r == 0 and s.has(g, NG):
                    t0 = s.at(g * GT, 2 * GT)
                    wait(sp, x_lo_done, s.groups(g), True)
                    sp.dma_start(xT_raw[:], xT_v[:, :, bass.ds(t0, GT)]).then_inc(xT_in, 16)
                    wait(sp, c_lo_done, s.groups(g), True)
                    sp.dma_start(cT_raw[:], cT_v[:, :, bass.ds(t0, GT)]).then_inc(cT_in, 16)
                g = (n - 4) // G
                if r == 0 and s.has(g, NG):
                    fill_stack(s, g, 0, (1,))
                if r == 1 and s.has(g, NG):
                    fill_stack(s, g, 1, (0,))
                b = n - LB - 1
                if s.has(b, NB):
                    for part in range(2):
                        wait(sp, shift_done, s.seqs(b + 1), True)
                        sp.dma_start(
                            stack_q[b // G % 2][SHIFT_ROW + part:SHIFT_ROW + part + 1, :, tok(b)],
                            shift[:, b % 2, part, :]).then_inc(shift_in[b % 2], 16)
                if r == 1 and s.has(g, NG):
                    fill_stack(s, g, 1, (1,))
                g = n // G
                if r == 3 and s.has(g, NG):
                    fill_stack(s, g, 0, (0,))
                g = (n - 12) // G
                if r == 0 and s.has(g, NG):
                    wait(sp, o_evac, s.seqs(G * (g + 1)), True)
                    wait(sp, den_ok_done, s.groups(g), True)
                    sp.dma_start(den[:], o_raw[g % 2][D:P:2 * D, :, :]).then_inc(den_in, 16)
                    wait(sp, o_lo_done, s.groups(g), True)
                    for w in range(HB):
                        a, u = w // 2, w % 2
                        sp.dma_start(o_all[D * w:D * w + D, :, :],
                                     o_raw[g % 2][2 * D * a:2 * D * a + D, 2 * u:2 * u + 2, :]).then_inc(num_in, 16)
                    wait(sp, z_done, s.seqs(G * (g - 1)), True)
                    sp.dma_start(x_rows[g % 2][:], x_v[:, bass.ds(s.at(G * g, RING), G), :]).then_inc(rows_in[g % 2], 16)
                g = (n - 13) // G
                if r == 1 and s.has(g, NG):
                    wait(sp, recip_done, s.groups(g + 1), True)
                    sp.dma_start(recip_dram[g % 2].rearrange("(p t) -> p t", p=P), recip[:]).then_inc(recip_out, 16)
                    wait(sp, recip_out, s.at(16 * (g + 1), 32), True)
                    wait(sp, mult_done, s.at(2 * g, 4), True)
                    for t in range(KT):
                        src = recip_dram[g % 2].rearrange("(w k t) -> k w t", k=KT, t=GT)[t]
                        sp.dma_start(recip_all[:, t, :],
                                     src.unsqueeze(1).to_broadcast([HB, D, GT])).then_inc(recip_in, 16)
                g = (n - 20) // G
                if r == 0 and s.has(g, NG):
                    wait(sp, norm_done, s.seqs(G * (g + 1)), True)
                    sp.dma_start(out_v[:, bass.ds(s.at(G * g, RING), G), :], z[g % 2][:]).then_inc(stored[g % 2], 16)

            run_slots(sp, slot)
            for j in range(2):
                sp.wait_ge(stored[j], 16 * NG // 2)

        @block.tensor
        def _(pe):
            pe.wait_ge(w_lo_done, 4)
            pe.wait_ge(bias_parts_in, 16)
            pe.wait_ge(pool_const, 3)
            pe.wait_ge(const_in, 16 * 8)
            splits = [(0, 0), (0, 1), (1, 0)]

            def project_qk(s, step):
                n, r = s.n, s.n % G
                g, t, tensor = n // G, r % 2, r // 2
                src = (xT_hi, xT_lo) if tensor == 0 else (cT_hi[g % 2], cT_lo[g % 2])
                if step == 0:
                    if r == 0:
                        wait(pe, x_lo_done, s.groups(g + 1))
                        wait(pe, c_lo_done, s.groups(g + 1))
                    wait(pe, qk_evac, s.seqs(n))
                for j in range(3 * step, 3 * step + 3):
                    k, (a, b) = j // 3, splits[j % 3]
                    mm = pe.matmul(qk_bank[:], (w_hi, w_lo)[b][tensor][:, k, t * P:(t + 1) * P],
                                   src[a][:, k, :], start=(j == 0), stop=(j == 5))
                if step == 1:
                    mm.then_inc(qk_ready, 1)

            def project_v(s):
                b = s.n - LV
                g = b // G
                src = (cT_hi[g % 2], cT_lo[g % 2])
                dst = v_bank[:, (b % 2) * H:(b % 2 + 1) * H]
                if b % 2 == 0:
                    wait(pe, v_evac, s.at(b // 2, RING // 2))
                pe.matmul(dst, ones_bf[0:3, :], bias_parts[:, 0:H], start=True, stop=False)
                for j in range(6):
                    k, (a, c) = j // 3, splits[j % 3]
                    mm = pe.matmul(dst, src[a][:, k, tok(b)], (w_hi, w_lo)[c][2][:, k, :],
                                   start=False, stop=(j == 5))
                mm.then_inc(v_ready, 1)

            def scores(s, c):
                b = s.n - LB
                g = b // G
                if c == 0 and b % 2 == 0:
                    use = g // 2 + 1
                    wait(pe, stack_in[g % 2][b % G // 2], s.at(16 * 25 * use, 16 * 25))
                wait(pe, max_done, s.chunks(NC * b + c - 1))
                for h in range(CH * c, CH * c + CH):
                    mm = pe.matmul(s_bank[c % 2][:, (h % CH) * P:(h % CH + 1) * P],
                                   stack_q[g % 2][0:MASK_END, h, tok(b)], stack_k[g % 2][0:MASK_END, h, tok(b)],
                                   start=True, stop=True)
                mm.then_inc(s_ready, 1)

            def scores_t(s, c):
                b = s.n - LC
                g = b // G
                if c == 0:
                    wait(pe, shift_in[b % 2], s.at(32 * (b // 2 + 1), 32 * RING // 2))
                wait(pe, exp_done, s.chunks(NC * b + c - 1))
                pe.matmul(st_bank[c % 2][:], id_bf[:], causal[:].unsqueeze(1).to_broadcast([P, CH, P]),
                          start=True, stop=False)
                for h in range(CH * c, CH * c + CH):
                    mm = pe.matmul(st_bank[c % 2][:, (h % CH) * P:(h % CH + 1) * P],
                                   stack_k[g % 2][0:MASK_ROW, h, tok(b)], stack_q[g % 2][0:MASK_ROW, h, tok(b)],
                                   start=False, stop=(h % CH == CH - 1))
                mm.then_inc(st_ready, 1)

            def weighted_v(s, b, c):
                wait(pe, exp_done, s.chunks(NC * b + c + 1))
                if c == 0:
                    wait(pe, o_evac, s.seqs(b))
                    if b % 2 == 0:
                        wait(pe, v_evac, s.at(b // 2 + 1, RING // 2))
                for j in range(CH):
                    mm = pe.matmul(pv_bank[2 * D * j:2 * D * (j + 1), c * P:(c + 1) * P],
                                   v_aug[:, b % RING, CH * c + j, :], probs[:, c, j * P:(j + 1) * P],
                                   start=True, stop=True)
                mm.then_inc(pv_ready, 1)

            def misc_free(s, before):
                n = s.n
                if before == "wo" and s.has(n - 1 - LW, NB):
                    wait(pe, z_done, s.seqs(n - LW))
                if before == "shift" and s.has(n - LB - 1, NB):
                    wait(pe, shift_done, s.seqs(n - LB))
                if before == "ksum" and n % G == 0 and s.has((n - 4) // G, NG):
                    wait(pe, key_bias_done, s.groups((n - 4) // G + 1))

            def slot(s):
                n, r = s.n, s.n % G
                for c in range(NC):
                    if s.has(n - LC, NB):
                        scores_t(s, c)
                    if s.has(n - LB, NB):
                        scores(s, c)
                    if c < 2 and s.has(n, NB):
                        project_qk(s, c)
                    if c == 1 and s.has(n - LB - 1, NB):
                        b = n - LB - 1
                        wait(pe, max_done, s.chunks(NC * (b + 1)))
                        misc_free(s, "wo")
                        pe.transpose(misc_bank[0:NH, 0:P], neg_max[:, b % 2, :], id_f32[:]).then_inc(shiftT_ready, 1)
                    if c == 2 and s.has(n - LV, NB):
                        project_v(s)
                    if c == 2 and r == 0 and s.has((n - 4) // G, NG):
                        g = (n - 4) // G
                        wait(pe, part1_done, s.at(2 * g + 2, 4))
                        misc_free(s, "wo")
                        misc_free(s, "shift")
                        for b in range(G):
                            for t in range(KT):
                                mm = pe.matmul(misc_bank[:, b:b + 1], parts[1][0][:, t, tok(b)], ones_bf[:, 0:1],
                                               start=(t == 0), stop=(t == KT - 1))
                        mm.then_inc(ksum_ready, 1)
                    if c == 3 and s.has(n - LW, NB):
                        b = n - LW
                        if b % G == 0:
                            wait(pe, o_lo_done, s.groups(b // G + 1))
                        misc_free(s, "wo")
                        misc_free(s, "shift")
                        misc_free(s, "ksum")
                        dst = misc_bank[:, 0:H]
                        pe.matmul(dst, ones_bf[0:3, :], bias_parts[:, H:2 * H], start=True, stop=False)
                        for j in range(6):
                            k, (a, m) = j // 3, splits[j % 3]
                            mm = pe.matmul(dst, (o_hi, o_lo)[a][:, k, tok(b)], (w_hi, w_lo)[m][3][:, k, :],
                                           start=False, stop=(j == 5))
                        mm.then_inc(wo_ready, 1)
                    b, cc = (n - LC, c - 2) if c >= 2 else (n - LC - 1, c + 2)
                    if s.has(b, NB):
                        weighted_v(s, b, cc)

            run_slots(pe, slot)

        @block.scalar
        def _(act):
            for j, raw in enumerate((proj, rest, o_all, recip_all)):
                act.wait_ge(w_in, 64)
                act.activation(w_hi[j][:], raw[:, :, 0:H], ACT.Copy).then_inc(w_hi_done, 1)

            def split_x(g, s):
                wait(act, xT_in, s.at(16 * (g + 1), 32))
                if g > 0:
                    wait(act, qk_ready, s.seqs(G * (g - 1) + 2))
                act.activation(xT_hi[:], xT_raw[:], ACT.Copy).then_inc(x_hi_done, 1)

            def split_c(g, s):
                wait(act, cT_in, s.at(16 * (g + 1), 32))
                if g > 1:
                    wait(act, v_ready, s.seqs(G * (g - 1)))
                    wait(act, qk_ready, s.seqs(G * (g - 1)))
                act.activation(cT_hi[g % 2][:], cT_raw[:], ACT.Copy).then_inc(c_hi_done, 1)

            split_x(0, Slot(0))
            split_c(0, Slot(0))
            act.wait_ge(const_in, 32)
            act.wait_ge(w_lo_done, 4)

            def slot(s):
                n, r = s.n, s.n % G
                for c in range(NC):
                    b = n - LC
                    if s.has(b, NB):
                        if c == 0 and b % G == 0:
                            wait(act, key_bias_done, s.groups(b // G + 1))
                        wait(act, st_ready, s.chunks(NC * b + c + 1))
                        wait(act, pv_ready, s.chunks(NC * (b - 1) + c + 1))
                        act.activation(probs[:, c, :], st_bank[c % 2][:], ACT.Exp,
                                       bias=key_bias[:, b % RING:b % RING + 1], scale=D ** -0.5).then_inc(exp_done, 1)
                    b = n - LC - 1
                    if c == 1 and s.has(b, NB):
                        g = b // G
                        wait(act, pv_ready, s.chunks(NC * (b + 1)))
                        if b % G == 0:
                            wait(act, den_in, s.at(16 * (g - 1), 32))
                            wait(act, num_in, s.at(16 * HB * (g - 1), 32 * HB))
                        act.activation(o_raw[g % 2][:, :, tok(b)], pv_bank[:].rearrange("p (c t) -> p c t", c=NC),
                                       ACT.Copy).then_inc(o_evac, 1)
                    if c == 1 and s.has(n, NB):
                        g, t, tensor = n // G, r % 2, r // 2
                        wait(act, qk_ready, s.seqs(n + 1))
                        if t == 0:
                            wait(act, part1_done, s.at(2 * g + tensor, 4))
                            wait(act, rest_done, s.at(2 * (2 * g + tensor), 8))
                        act.activation(proj[:, t, :], qk_bank[:], ACT.Relu,
                                       bias=bias_qk[:, tensor, t:t + 1]).then_inc(qk_evac, 1)
                    g = (n - 14) // G
                    if c == 1 and r == 2 and s.has(g, NG):
                        wait(act, mult_done, s.at(2 * (g + 1), 4))
                        wait(act, wo_ready, s.seqs(G * g))
                        act.activation(o_hi[:], o_all[:], ACT.Copy).then_inc(o_hi_done, 1)
                    g = n // G + 1
                    if c == 2 and r == 2 and s.has(g, NG):
                        split_x(g, s)
                    if c == 3 and r == 2 and s.has(g, NG):
                        split_c(g, s)
                    b = n - LV
                    if c == 3 and b % 2 == 1 and s.has(b, NB):
                        wait(act, v_ready, s.seqs(b + 1))
                        wait(act, pv_ready, s.chunks(NC * (b - RING + 1)))
                        act.activation(v_aug[:, (b - 1) % RING:(b - 1) % RING + 2, :, 0:D],
                                       v_bank[:].rearrange("p (b h d) -> p b h d", b=2, d=D),
                                       ACT.Relu).then_inc(v_evac, 1)
                    g = (n - 19) // G
                    if r == 3 and s.has(g, NG):
                        wait(act, scale_done, s.groups(g + 1))
                        act.activation(z[g % 2][:, c, :], z[g % 2][:, c, :], ACT.Identity,
                                       bias=neg_mean_rstd[:, c:c + 1], scale=rstd[:, c:c + 1]).then_inc(norm_done, 1)

            run_slots(act, slot)

        @block.vector
        def _(dve):
            dve.memset(zeros_bf[:], 0.0)
            dve.wait_ge(bias_in, 16)
            dve.tensor_copy(bias_parts1[:, 0, :], bias_row).then_inc(bias_step, 1)
            dve.wait_ge(bias_step, 1)
            dve.tensor_tensor(bias_rest, bias_row, bias_parts1[:, 0, :], ALU.subtract).then_inc(bias_step, 1)
            dve.wait_ge(bias_step, 2)
            dve.tensor_copy(bias_parts1[:, 1, :], bias_rest).then_inc(bias_step, 1)
            dve.wait_ge(bias_step, 3)
            dve.tensor_tensor(bias_parts1[:, 2, :], bias_rest, bias_parts1[:, 1, :], ALU.subtract).then_inc(bias_step, 1)
            dve.wait_ge(mask_in, 32)
            dve.tensor_copy(masks_bf[:], masks_f).then_inc(masks_done, 1)
            for j, raw in enumerate((proj, rest, o_all, recip_all)):
                dve.wait_ge(w_hi_done, j + 1)
                dve.tensor_tensor(w_lo[j][:], raw[:, :, 0:H], w_hi[j][:].bitcast(F32), ALU.subtract).then_inc(w_lo_done, 1)

            def first_part(s, g, tensor):
                i = 2 * g + tensor
                wait(dve, qk_evac, s.seqs(G * g + 2 * tensor + 2))
                for h in range(2):
                    wait(dve, stack_in[(g - 1) % 2][h], s.at(16 * 25 * ((g - 1) // 2 + 1), 16 * 25))
                if tensor == 1:
                    wait(dve, ksum_ready, s.groups(g))
                dve.tensor_copy(parts[tensor][0][:], proj[:]).then_inc(part1_done, 1)

            def second_part(s, g, tensor):
                i = 2 * g + tensor
                wait(dve, rest_done, s.at(2 * (i + 1), 8))
                dve.tensor_copy(parts[tensor][1][:], rest[:]).then_inc(part2_done, 1)

            def slot(s):
                n, r = s.n, s.n % G
                for c in range(NC):
                    b = n - LB
                    if s.has(b, NB):
                        wait(dve, s_ready, s.chunks(NC * b + c + 1))
                        if c == 0:
                            wait(dve, shiftT_ready, s.seqs(b - 1))
                        dve.tensor_reduce(neg_max[:, b % 2, CH * c:CH * c + CH],
                                          s_bank[c % 2][:].rearrange("p (h k) -> p h k", k=P),
                                          AX.X, ALU.max, negate=True).then_inc(max_done, 1)
                    b = n - 1 - LW
                    if c == 0 and s.has(b, NB):
                        g = b // G
                        wait(dve, wo_ready, s.seqs(b + 1))
                        if b % G == 0:
                            wait(dve, rows_in[g % 2], s.at(16 * (g // 2 + 1), 16))
                            wait(dve, stored[g % 2], s.at(16 * (g // 2), 16))
                        dve.scalar_tensor_tensor(z[g % 2][:, b % G, :], misc_bank[:, 0:H], 0.0, x_rows[g % 2][:, b % G, :],
                                                 ALU.max, ALU.add).then_inc(z_done, 1)
                        wait(dve, z_done, s.seqs(b + 1))
                        wait(dve, aggr_done, s.seqs(b))
                        dve.bn_stats(stats[:], z[g % 2][:, b % G, :]).then_inc(stats_done, 1)
                        wait(dve, stats_done, s.seqs(b + 1), True)
                        dve.bn_aggr(mean_var[:, g % 2, b % G, :], stats[:]).then_inc(aggr_done, 1)
                    g = (n - 18) // G
                    if c == 0 and r == 2 and s.has(g, NG):
                        wait(dve, aggr_done, s.seqs(G * (g + 1)))
                        wait(dve, std_done, s.groups(g))
                        dve.tensor_scalar(var_n1[:], mean_var[:, g % 2, :, 1], float(H) / (H - 1), None,
                                          ALU.mult).then_inc(var_done, 1)
                    b = n - LB - 1
                    if c == 1 and s.has(b, NB):
                        wait(dve, shiftT_ready, s.seqs(b + 1))
                        wait(dve, shift_in[b % 2], s.at(32 * (b // 2), 32 * RING // 2))
                        dve.tensor_copy(shift[:, b % 2, 0, :], misc_bank[0:NH, 0:P]).then_inc(shift1_done, 1)
                        wait(dve, shift1_done, s.seqs(b + 1))
                        dve.tensor_tensor(shift[:, b % 2, 1, :], misc_bank[0:NH, 0:P], shift[:, b % 2, 0, :],
                                          ALU.subtract).then_inc(shift_done, 1)
                    if c == 1 and r == 2 and s.has(g, NG):
                        wait(dve, std_done, s.groups(g + 1))
                        dve.tensor_scalar(std_eps[:], std[:], EPS, None, ALU.add).then_inc(std_eps_done, 1)
                        wait(dve, std_eps_done, s.groups(g + 1))
                        wait(dve, norm_done, s.seqs(G * g))
                        dve.reciprocal(rstd[:], std_eps[:]).then_inc(rstd_done, 1)
                        wait(dve, rstd_done, s.groups(g + 1))
                        dve.scalar_tensor_tensor(neg_mean_rstd[:], mean_var[:, g % 2, :, 0], -1.0, rstd[:],
                                                 ALU.mult, ALU.mult).then_inc(scale_done, 1)
                    g = (n - 4) // G
                    if c == 2 and r == 0 and s.has(g, NG):
                        wait(dve, ksum_ready, s.groups(g + 1))
                        wait(dve, exp_done, s.chunks(NC * G * (g - 1)))
                        dve.tensor_scalar(key_bias[:, G * (g % 2):G * (g % 2) + G], misc_bank[:, 0:G], 0.0, -1e30,
                                          ALU.is_equal, ALU.mult).then_inc(key_bias_done, 1)
                        second_part(s, g, 1)
                    g = (n - 14) // G
                    if c == 2 and r == 2 and s.has(g, NG):
                        wait(dve, o_hi_done, s.groups(g + 1))
                        dve.tensor_tensor(o_lo[:], o_all[:], o_hi[:].bitcast(F32), ALU.subtract).then_inc(o_lo_done, 1)
                    g = (n - 12) // G
                    if c == 3 and r == 0 and s.has(g, NG):
                        wait(dve, den_in, s.at(16 * (g + 1), 32))
                        wait(dve, recip_done, s.groups(g))
                        dve.tensor_scalar(den_ok[:], den[:], 1e-30, None, ALU.max).then_inc(den_ok_done, 1)
                        wait(dve, den_ok_done, s.groups(g + 1))
                        wait(dve, recip_out, s.at(16 * g, 32))
                        dve.reciprocal(recip[:], den_ok[:]).then_inc(recip_done, 1)
                    g = n // G
                    if c == 3 and r == 1 and s.has(g, NG):
                        first_part(s, g, 0)
                    if c == 3 and r == 2 and s.has(g, NG):
                        second_part(s, g, 0)
                    if c == 3 and r == 3 and s.has(g, NG):
                        first_part(s, g, 1)

            run_slots(dve, slot)

        @block.gpsimd
        def _(pool):
            pool.memset(ones_bf[:], 1.0)
            pool.memset(half[:], 0.5)
            pool.memset(id_bf[:], 0.0)
            pool.memset(causal[:], 0.0)
            pool.memset(v_aug[:], 1.0).then_inc(pool_const, 1)
            pool.wait_ge(pool_const, 1)
            pool.affine_select(out=id_bf[:], in_=id_bf[:], compare_op=ALU.not_equal, fill=1.0, base=0,
                               pattern=[[-1, P]], channel_multiplier=1).then_inc(pool_const, 1)
            pool.affine_select(out=causal[:], in_=causal[:], compare_op=ALU.is_ge, fill=-1e30, base=0,
                               pattern=[[1, P]], channel_multiplier=-1).then_inc(pool_const, 1)
            pool.wait_ge(w_lo_done, 4)

            def split_x(g, s):
                wait(pool, x_hi_done, s.groups(g + 1))
                pool.tensor_tensor(xT_lo[:], xT_raw[:], xT_hi[:].bitcast(F32), ALU.subtract).then_inc(x_lo_done, 1)

            def split_c(g, s):
                wait(pool, c_hi_done, s.groups(g + 1))
                pool.tensor_tensor(cT_lo[g % 2][:], cT_raw[:], cT_hi[g % 2][:].bitcast(F32),
                                   ALU.subtract).then_inc(c_lo_done, 1)

            split_x(0, Slot(0))
            split_c(0, Slot(0))

            def rest_half(s, g, tensor, t):
                i = 2 * g + tensor
                if t == 0:
                    wait(pool, part1_done, s.at(i + 1, 4))
                    wait(pool, part3_done, s.at(2 * i, 8))
                    wait(pool, part2_done, s.at(i, 4))
                pool.tensor_tensor(rest[:, t, :], proj[:, t, :], parts[tensor][0][:, t, :],
                                   ALU.subtract).then_inc(rest_done, 1)

            def third_half(s, g, tensor, t):
                i = 2 * g + tensor
                if t == 0:
                    wait(pool, part2_done, s.at(i + 1, 4))
                pool.tensor_tensor(parts[tensor][2][:, t, :], rest[:, t, :], parts[tensor][1][:, t, :],
                                   ALU.subtract).then_inc(part3_done, 1)

            def normalise_half(s, g, t):
                if t == 0:
                    wait(pool, num_in, s.at(16 * HB * (g + 1), 32 * HB))
                    wait(pool, recip_in, s.at(32 * (g + 1), 64))
                pool.tensor_tensor(o_all[:, t, :], o_all[:, t, :], recip_all[:, t, :], ALU.mult).then_inc(mult_done, 1)

            def slot(s):
                n, r = s.n, s.n % G
                for c in range(NC):
                    g = (n - 4) // G
                    if r == 0 and s.has(g, NG):
                        if c < 2:
                            rest_half(s, g, 1, c)
                        if c == 3:
                            third_half(s, g, 1, 0)
                    if r == 1 and c == 0 and s.has(g, NG):
                        third_half(s, g, 1, 1)
                    g = n // G
                    if r == 2 and c < 2 and s.has(g, NG):
                        rest_half(s, g, 0, c)
                    if r == 3 and c < 2 and s.has(g, NG):
                        third_half(s, g, 0, c)
                    if r == 3 and s.has(g + 1, NG):
                        if c == 2:
                            split_x(g + 1, s)
                        if c == 3:
                            split_c(g + 1, s)
                    g = (n - 13) // G
                    if r == 1 and c == 3 and s.has(g, NG):
                        normalise_half(s, g, 0)
                    g = (n - 14) // G
                    if r == 2 and c == 0 and s.has(g, NG):
                        normalise_half(s, g, 1)
                    g = (n - 18) // G
                    if r == 2 and c == 1 and s.has(g, NG):
                        wait(pool, var_done, s.groups(g + 1))
                        wait(pool, std_eps_done, s.groups(g))
                        pool.tensor_tensor(std[:], var_n1[:], half[:], ALU.pow).then_inc(std_done, 1)

            run_slots(pool, slot)


def kernel(x, ctx_1024, L0_xattn_Wq, L0_xattn_bq, L0_xattn_Wk, L0_xattn_bk, L0_xattn_Wv, L0_xattn_bv,
           L0_xattn_Wo, L0_xattn_bo):
    import concourse.bacc as bacc
    from concourse.bass_utils import run_bass_kernel_spmd

    x, c = np.asarray(x), np.asarray(ctx_1024)
    feature = np.arange(H).reshape(KT, HB, D).transpose(0, 2, 1).reshape(H)
    head = np.array([[4 * (2 * (w % 2) + t) + w // 2 for w in range(HB)] for t in range(KT)])
    wo_rows = (head[:, :, None] * D + np.arange(D)).reshape(H)

    q = np.arange(P)
    block = np.arange(MASK_N)[:, None]
    inside = (q // MASK_W == block)
    mask_q = np.where(inside, 2.0 ** (-24 * (q % MASK_W)), 0.0).astype(np.float32)
    mask_k = np.where(inside, -(2.0 ** (24 * (q % MASK_W) + 7)), np.where(q // MASK_W > block, -(2.0 ** 127), 0.0))
    arrays = {
        "xT": np.ascontiguousarray(x.reshape(NB * P, H).T),
        "cT": np.ascontiguousarray(c.reshape(NB * P, H).T),
        "x": np.ascontiguousarray(x),
        "wq": np.ascontiguousarray(np.asarray(L0_xattn_Wq)[:, feature]),
        "wk": np.ascontiguousarray(np.asarray(L0_xattn_Wk)[:, feature]),
        "wv": np.ascontiguousarray(np.asarray(L0_xattn_Wv)),
        "wo": np.ascontiguousarray(np.asarray(L0_xattn_Wo)[wo_rows]),
        "bqk": np.ascontiguousarray(np.stack([np.asarray(b)[feature].reshape(KT, P).T
                                              for b in (L0_xattn_bq, L0_xattn_bk)], axis=1)),
        "bvo": np.ascontiguousarray(np.concatenate([np.asarray(L0_xattn_bv), np.asarray(L0_xattn_bo)])[None, :]),
        "ident": np.eye(P, dtype=np.float32),
        "mask_q": mask_q,
        "mask_k": mask_k.astype(np.float32),
    }
    nc = bacc.Bacc("TRN2", target_bir_lowering=False, num_devices=1,
                   dynamic_dma_scratch_size=1024)
    args = [nc.dram_tensor(name, a.shape, F32, kind="ExternalInput").ap() for name, a in arrays.items()]
    out = nc.dram_tensor("out", (NB, P, H), F32, kind="ExternalOutput").ap()
    build(nc, *args, out)
    r = run_bass_kernel_spmd(nc, [arrays], core_ids=[0])
    return r.results[0]["out"]
```

```python
from contextlib import ExitStack

import numpy as np
import concourse.bass as bass
import concourse.mybir as mybir
from concourse.alu_op_type import AluOpType as ALU

F32 = mybir.dt.float32
F32R = mybir.dt.float32r
BF16 = mybir.dt.bfloat16
ACT = mybir.ActivationFunctionType
AX = mybir.AxisListType

P = 128
NB = 128
H = 256
KT = H // P
NH = 16
D = H // NH
G = 4
NG = NB // G
GT = G * P
CH = 4
NC = NH // CH
HB = 8
SLOTS = 6
SHIFT_ROW = SLOTS * D
MASK_ROW = SHIFT_ROW + 2
MASK_W = 5
MASK_N = -(-P // MASK_W)
MASK_END = MASK_ROW + MASK_N
Q_PARTS = (0, 0, 0, 1, 1, 2)
K_PARTS = (0, 1, 2, 0, 1, 0)
STACK_DMAS = 2 * SLOTS + 1
EPS = 1e-8

LV = 2
LB = 7
LC = 9
LW = 16
RING = 8
SLOT_END = 152
LOOP_FROM, LOOP_TO = 24, 120


class Slot:

    def __init__(self, n, i=None):
        self.n, self.i = n, i

    def at(self, value, per_iteration):
        if self.i is None:
            return value
        assert value > 0
        return value + per_iteration * self.i

    def chunks(self, value):
        return self.at(value, RING * NC)

    def seqs(self, value):
        return self.at(value, RING)

    def groups(self, value):
        return self.at(value, RING // G)

    def has(self, index, total):
        return 0 <= index < total


def wait(eng, sem, value, alone=False):
    if not isinstance(value, int) or value > 0:
        eng.wait_ge(sem, value)
        if alone and not isinstance(value, int):
            eng.nop(nofuse=True)


def run_slots(eng, body):
    for n in range(LOOP_FROM):
        body(Slot(n))
    with eng.Fori(0, (LOOP_TO - LOOP_FROM) // RING) as i:
        for k in range(RING):
            body(Slot(LOOP_FROM + k, i))
    for n in range(LOOP_TO, SLOT_END):
        body(Slot(n))


def build(nc, xT, cT, x, wq, wk, wv, wo, bqk, bvo, ident, mask_q, mask_k, out):
    xT_v = xT.rearrange("(k p) t -> p k t", p=P)
    cT_v = cT.rearrange("(k p) t -> p k t", p=P)
    x_v = x.rearrange("b q f -> q b f")
    out_v = out.rearrange("b q f -> q b f")
    recip_dram = nc.dram_tensor("recip_dram", (2, NH * GT), F32, kind="Internal").ap()

    with ExitStack() as ctx:
        def sb(name, shape, dt=F32):
            return ctx.enter_context(nc.sbuf_tensor(name, shape, dt))

        def sem(name):
            return ctx.enter_context(nc.semaphore(name))

        def bank(name):
            return ctx.enter_context(nc.psum_tensor(name, [P, 512], F32))

        w_hi = [sb(f"w_hi{j}", [P, KT, H], F32R) for j in range(4)]
        w_lo = [sb(f"w_lo{j}", [P, KT, H], F32R) for j in range(4)]
        bias_qk = sb("bias_qk", [P, 2, KT])
        bias_parts = sb("bias_parts", [3, 2 * H], BF16)
        id_f32 = sb("id_f32", [P, P])
        ones_bf = sb("ones_bf", [P, P], BF16)
        zeros_bf = sb("zeros_bf", [2, GT], BF16)
        masks_bf = sb("masks_bf", [MASK_N, 2, P], BF16)
        half = sb("half", [P, G])
        id_bf = sb("id_bf", [P, P], BF16)
        causal = sb("causal", [P, P], BF16)
        xT_raw = sb("xT_raw", [P, KT, GT])
        cT_raw = sb("cT_raw", [P, KT, GT])
        xT_hi = sb("xT_hi", [P, KT, GT], F32R)
        xT_lo = sb("xT_lo", [P, KT, GT], F32R)
        cT_hi = [sb(f"cT_hi{j}", [P, KT, GT], F32R) for j in range(2)]
        cT_lo = [sb(f"cT_lo{j}", [P, KT, GT], F32R) for j in range(2)]
        x_rows = [sb(f"x_rows{j}", [P, G, H]) for j in range(2)]
        proj = [sb(f"proj{j}", [P, KT, GT]) for j in range(2)]
        rest = sb("rest", [P, KT, GT])
        parts = [[sb(f"part{m}_{j}", [P, KT, GT], BF16) for m in range(3)] for j in range(2)]
        stack_q = [sb(f"stack_q{j}", [P, NH, GT], BF16) for j in range(2)]
        stack_k = [sb(f"stack_k{j}", [P, NH, GT], BF16) for j in range(2)]
        v_aug = sb("v_aug", [P, RING, NH, 2 * D])
        neg_max = sb("neg_max", [P, 2, NH])
        shift_parts = sb("shift_parts", [P, 2, 2, NH], BF16)
        shift = sb("shift", [2 * NH, 2, P], BF16)
        key_bias = sb("key_bias", [P, RING])
        probs = sb("probs", [P, 4, CH * P])
        o_raw = [sb(f"o_raw{j}", [P, NC, GT]) for j in range(2)]
        den = sb("den", [P, 64])
        den_ok = sb("den_ok", [P, 64])
        recip = sb("recip", [P, 64])
        o_all = sb("o_all", [P, KT, GT])
        recip_all = sb("recip_all", [P, KT, GT])
        o_hi = sb("o_hi", [P, KT, GT], F32R)
        o_lo = sb("o_lo", [P, KT, GT], F32R)
        z = [sb(f"z{j}", [P, G, H]) for j in range(2)]
        bias_row = z[0][0:1, 0:2, :].rearrange("p a f -> p (a f)")
        bias_rest = z[0][0:1, 2:4, :].rearrange("p a f -> p (a f)")
        bias_parts1 = stack_q[0][0:1, 0:3, :]
        masks_f = z[1][0:MASK_N, 0, :].rearrange("p (a t) -> p a t", a=2)
        stats = sb("stats", [P, 6])
        mean_var = sb("mean_var", [P, 2, G, 2])
        var_n1 = sb("var_n1", [P, G])
        std = sb("std", [P, G])
        std_eps = sb("std_eps", [P, G])
        rstd = sb("rstd", [P, G])
        neg_mean_rstd = sb("neg_mean_rstd", [P, G])

        s_bank = [bank(f"s_bank{j}") for j in range(2)]
        st_bank = [bank(f"st_bank{j}") for j in range(2)]
        pv_bank = bank("pv_bank")
        qk_bank = bank("qk_bank")
        v_bank = bank("v_bank")
        misc_bank = bank("misc_bank")

        w_in = sem("w_in")
        const_in = sem("const_in")
        mask_in = sem("mask_in")
        bias_in = sem("bias_in")
        bias_parts_in = sem("bias_parts_in")
        xT_in = sem("xT_in")
        cT_in = sem("cT_in")
        rows_in = [sem(f"rows_in{j}") for j in range(2)]
        stack_in = [sem(f"stack_in{j}") for j in range(2)]
        shift_in = [sem(f"shift_in{j}") for j in range(2)]
        den_in = sem("den_in")
        num_in = sem("num_in")
        recip_out = sem("recip_out")
        recip_in = sem("recip_in")
        stored = [sem(f"stored{j}") for j in range(2)]
        w_hi_done = sem("w_hi_done")
        w_lo_done = sem("w_lo_done")
        bias_step = sem("bias_step")
        masks_done = sem("masks_done")
        pool_const = sem("pool_const")
        qk_ready = sem("qk_ready")
        v_ready = sem("v_ready")
        s_ready = sem("s_ready")
        st_ready = sem("st_ready")
        pv_ready = sem("pv_ready")
        shiftT_ready = sem("shiftT_ready")
        ksum_ready = sem("ksum_ready")
        wo_ready = sem("wo_ready")
        qk_evac = sem("qk_evac")
        v_evac = sem("v_evac")
        exp_done = sem("exp_done")
        o_evac = sem("o_evac")
        x_hi_done = sem("x_hi_done")
        c_hi_done = sem("c_hi_done")
        o_hi_done = sem("o_hi_done")
        norm_done = sem("norm_done")
        max_done = sem("max_done")
        part_a_done = sem("part_a_done")
        parts_done = sem("parts_done")
        shift_done = sem("shift_done")
        key_bias_done = sem("key_bias_done")
        part1_done = sem("part1_done")
        part2_done = sem("part2_done")
        x_lo_done = sem("x_lo_done")
        c_lo_done = sem("c_lo_done")
        o_lo_done = sem("o_lo_done")
        den_ok_done = sem("den_ok_done")
        recip_done = sem("recip_done")
        z_done = sem("z_done")
        stats_done = sem("stats_done")
        aggr_done = sem("aggr_done")
        var_done = sem("var_done")
        std_eps_done = sem("std_eps_done")
        rstd_done = sem("rstd_done")
        scale_done = sem("scale_done")
        rest_done = sem("rest_done")
        part3_done = sem("part3_done")
        mult_done = sem("mult_done")
        std_done = sem("std_done")

        block = ctx.enter_context(nc.Block())

        def tok(b):
            return slice((b % G) * P, (b % G) * P + P)

        @block.sync
        def _(sp):
            sp.dma_start(id_f32[:], ident).then_inc(const_in, 16)
            sp.dma_start(bias_qk[:], bqk).then_inc(const_in, 16)
            sp.dma_start(bias_row, bvo).then_inc(bias_in, 16)
            sp.dma_start(masks_f[:, 0, :], mask_q).then_inc(mask_in, 16)
            sp.dma_start(masks_f[:, 1, :], mask_k).then_inc(mask_in, 16)
            for j, (w, raw) in enumerate(zip((wq, wk, wv, wo), (proj[0], rest, o_all, recip_all))):
                sp.dma_start(raw[:, :, 0:H], w.rearrange("(k p) f -> p k f", p=P)).then_inc(w_in, 16)
            sp.wait_ge(bias_step, 4)
            sp.dma_start(bias_parts[:], bias_parts1.rearrange("a m f -> a (m f)")).then_inc(bias_parts_in, 16)
            sp.wait_ge(masks_done, 1)
            for j in range(2):
                for m, stack in enumerate((stack_q[j], stack_k[j])):
                    dst = stack[MASK_ROW:MASK_END, :, :].rearrange("p h (b t) -> p (h b) t", t=P)
                    src = masks_bf[:, m, :].unsqueeze(1).to_broadcast([MASK_N, NH * G, P])
                    sp.dma_start(dst, src).then_inc(const_in, 16)
            sp.wait_ge(pool_const, 1)
            for j in range(2):
                dst = stack_k[j][SHIFT_ROW:MASK_ROW, :, :].rearrange("p h (b t) -> p (h b) t", t=P)
                src = ones_bf[0:2, :].unsqueeze(1).to_broadcast([2, NH * G, P])
                sp.dma_start(dst, src).then_inc(const_in, 16)
            sp.dma_start(xT_raw[:], xT_v[:, :, 0:GT]).then_inc(xT_in, 16)
            sp.dma_start(cT_raw[:], cT_v[:, :, 0:GT]).then_inc(cT_in, 16)

            def fill_stack(s, g, tensor):
                stack = (stack_q, stack_k)[tensor][g % 2]
                wait(sp, part3_done, s.at(2 * (2 * g + tensor + 1), 8), True)
                wait(sp, st_ready, s.chunks(NC * G * (g - 1)), True)
                for slot, part in enumerate((Q_PARTS, K_PARTS)[tensor]):
                    sp.dma_start(stack[D * slot:D * slot + D, :, :], parts[tensor][part][:]).then_inc(stack_in[g % 2], 16)
                if tensor == 0:
                    src = zeros_bf[:, :].unsqueeze(1).to_broadcast([2, NH, GT])
                    sp.dma_start(stack[SHIFT_ROW:MASK_ROW, :, :], src).then_inc(stack_in[g % 2], 16)

            def slot(s):
                n, r = s.n, s.n % G
                g = n // G + 1
                if r == 0 and s.has(g, NG):
                    t0 = s.at(g * GT, 2 * GT)
                    wait(sp, x_lo_done, s.groups(g), True)
                    sp.dma_start(xT_raw[:], xT_v[:, :, bass.ds(t0, GT)]).then_inc(xT_in, 16)
                    wait(sp, c_lo_done, s.groups(g), True)
                    sp.dma_start(cT_raw[:], cT_v[:, :, bass.ds(t0, GT)]).then_inc(cT_in, 16)
                g = (n - 5) // G
                if r == 1 and s.has(g, NG):
                    fill_stack(s, g, 0)
                g = (n - 15) // G
                if r == 3 and s.has(g, NG):
                    wait(sp, recip_out, s.at(16 * (g + 1), 32), True)
                    wait(sp, mult_done, s.at(2 * g, 4), True)
                    for a in range(CH):
                        src = recip_dram[g % 2].rearrange("(a r) -> a r", a=CH)[a]
                        sp.dma_start(recip_all[P // 2 * (a % 2):P // 2 * (a % 2 + 1), a // 2, :],
                                     src.unsqueeze(0).to_broadcast([D, NC * GT])).then_inc(recip_in, 16)
                b = n - LB - 1
                if s.has(b, NB):
                    wait(sp, shift_done, s.seqs(b + 1), True)
                    sp.dma_start(stack_q[b // G % 2][SHIFT_ROW:MASK_ROW, :, tok(b)],
                                 shift[:, b % 2, :]).then_inc(shift_in[b % 2], 16)
                g = (n - 12) // G
                if r == 0 and s.has(g, NG):
                    wait(sp, z_done, s.seqs(G * (g - 1)), True)
                    sp.dma_start(x_rows[g % 2][:], x_v[:, bass.ds(s.at(G * g, RING), G), :]).then_inc(rows_in[g % 2], 16)
                g = (n - 13) // G
                if r == 1 and s.has(g, NG):
                    wait(sp, o_evac, s.seqs(G * (g + 1)), True)
                    wait(sp, den_ok_done, s.groups(g), True)
                    sp.dma_start(den[:], o_raw[g % 2][D:P:2 * D, :, :]).then_inc(den_in, 16)
                g = (n - 5) // G
                if r == 1 and s.has(g, NG):
                    fill_stack(s, g, 1)
                g = (n - 14) // G
                if r == 2 and s.has(g, NG):
                    wait(sp, recip_done, s.groups(g + 1), True)
                    sp.dma_start(recip_dram[g % 2].rearrange("(p t) -> p t", p=P), recip[:]).then_inc(recip_out, 16)
                    wait(sp, o_lo_done, s.groups(g), True)
                    for a in range(CH):
                        sp.dma_start(o_all[P // 2 * (a % 2):P // 2 * (a % 2 + 1), a // 2, :],
                                     o_raw[g % 2][2 * D * a:2 * D * a + D, :, :]).then_inc(num_in, 16)
                g = (n - 22) // G
                if r == 2 and s.has(g, NG):
                    wait(sp, norm_done, s.seqs(G * (g + 1)), True)
                    sp.dma_start(out_v[:, bass.ds(s.at(G * g, RING), G), :], z[g % 2][:]).then_inc(stored[g % 2], 16)

            run_slots(sp, slot)
            for j in range(2):
                sp.wait_ge(stored[j], 16 * NG // 2)

        @block.tensor
        def _(pe):
            pe.wait_ge(w_lo_done, 4)
            pe.wait_ge(bias_parts_in, 16)
            pe.wait_ge(pool_const, 3)
            pe.wait_ge(const_in, 16 * 8)
            splits = [(0, 0), (0, 1), (1, 0)]

            def project_qk(s, step):
                n, r = s.n, s.n % G
                g, t, tensor = n // G, r % 2, r // 2
                src = (xT_hi, xT_lo) if tensor == 0 else (cT_hi[g % 2], cT_lo[g % 2])
                if step == 0:
                    if r == 0:
                        wait(pe, x_lo_done, s.groups(g + 1))
                        wait(pe, c_lo_done, s.groups(g + 1))
                    wait(pe, qk_evac, s.seqs(n))
                for j in range(3 * step, 3 * step + 3):
                    k, (a, b) = j // 3, splits[j % 3]
                    mm = pe.matmul(qk_bank[:], (w_hi, w_lo)[b][tensor][:, k, t * P:(t + 1) * P],
                                   src[a][:, k, :], start=(j == 0), stop=(j == 5))
                if step == 1:
                    mm.then_inc(qk_ready, 1)

            def project_v(s):
                b = s.n - LV
                g = b // G
                src = (cT_hi[g % 2], cT_lo[g % 2])
                dst = v_bank[:, (b % 2) * H:(b % 2 + 1) * H]
                if b % 2 == 0:
                    wait(pe, v_evac, s.at(b // 2, RING // 2))
                pe.matmul(dst, ones_bf[0:3, :], bias_parts[:, 0:H], start=True, stop=False)
                for j in range(6):
                    k, (a, c) = j // 3, splits[j % 3]
                    mm = pe.matmul(dst, src[a][:, k, tok(b)], (w_hi, w_lo)[c][2][:, k, :],
                                   start=False, stop=(j == 5))
                mm.then_inc(v_ready, 1)

            def scores(s, c):
                b = s.n - LB
                g = b // G
                if c == 0 and b % G == 0:
                    wait(pe, stack_in[g % 2], s.at(16 * STACK_DMAS * (g // 2 + 1), 16 * STACK_DMAS))
                wait(pe, max_done, s.chunks(NC * b + c - 1))
                for h in range(CH * c, CH * c + CH):
                    mm = pe.matmul(s_bank[c % 2][:, (h % CH) * P:(h % CH + 1) * P],
                                   stack_q[g % 2][0:MASK_END, h, tok(b)], stack_k[g % 2][0:MASK_END, h, tok(b)],
                                   start=True, stop=True)
                mm.then_inc(s_ready, 1)

            def scores_t(s, c):
                b = s.n - LC
                g = b // G
                if c == 0:
                    wait(pe, shift_in[b % 2], s.at(16 * (b // 2 + 1), 16 * RING // 2))
                wait(pe, exp_done, s.chunks(NC * b + c - 1))
                pe.matmul(st_bank[c % 2][:], id_bf[:], causal[:].unsqueeze(1).to_broadcast([P, CH, P]),
                          start=True, stop=False)
                for h in range(CH * c, CH * c + CH):
                    mm = pe.matmul(st_bank[c % 2][:, (h % CH) * P:(h % CH + 1) * P],
                                   stack_k[g % 2][0:MASK_ROW, h, tok(b)], stack_q[g % 2][0:MASK_ROW, h, tok(b)],
                                   start=False, stop=(h % CH == CH - 1))
                mm.then_inc(st_ready, 1)

            def weighted_v(s, b, c):
                wait(pe, exp_done, s.chunks(NC * b + c + 1))
                if c == 0:
                    wait(pe, o_evac, s.seqs(b))
                    if b % 2 == 0:
                        wait(pe, v_evac, s.at(b // 2 + 1, RING // 2))
                for j in range(CH):
                    mm = pe.matmul(pv_bank[2 * D * j:2 * D * (j + 1), c * P:(c + 1) * P],
                                   v_aug[:, b % RING, CH * c + j, :], probs[:, c, j * P:(j + 1) * P],
                                   start=True, stop=True)
                mm.then_inc(pv_ready, 1)

            def misc_free(s, before):
                n = s.n
                if before == "last slot's":
                    if s.has(n - 1 - LW, NB):
                        wait(pe, z_done, s.seqs(n - LW))
                    if n % G == 1 and s.has((n - 5) // G, NG):
                        wait(pe, key_bias_done, s.groups((n - 5) // G + 1))
                if before == "shift" and s.has(n - LB - 1, NB):
                    wait(pe, shift_done, s.seqs(n - LB))
                if before == "rows" and s.has(n - LW, NB):
                    wait(pe, z_done, s.seqs(n - LW + 1))

            def slot(s):
                n, r = s.n, s.n % G
                for c in range(NC):
                    if s.has(n - LC, NB):
                        scores_t(s, c)
                    if s.has(n - LB, NB):
                        scores(s, c)
                    if c < 2 and s.has(n, NB):
                        project_qk(s, c)
                    b = n - LB - 1
                    if c == 0 and s.has(b, NB):
                        wait(pe, parts_done, s.seqs(b + 1))
                        misc_free(s, "last slot's")
                        pe.transpose(misc_bank[:].bitcast(BF16)[0:2 * NH, 0:P],
                                     shift_parts[:, b % 2, :, :].rearrange("p m h -> p (m h)"), id_bf[:]).then_inc(shiftT_ready, 1)
                    b = n - LW
                    if c == 2 and s.has(b, NB):
                        if b % G == 0:
                            wait(pe, o_lo_done, s.groups(b // G + 1))
                        misc_free(s, "last slot's")
                        misc_free(s, "shift")
                        dst = misc_bank[:, 0:H]
                        pe.matmul(dst, ones_bf[0:3, :], bias_parts[:, H:2 * H], start=True, stop=False)
                        for j in range(6):
                            k, (a, m) = j // 3, splits[j % 3]
                            mm = pe.matmul(dst, (o_hi, o_lo)[a][:, k, tok(b)], (w_hi, w_lo)[m][3][:, k, :],
                                           start=False, stop=(j == 5))
                        mm.then_inc(wo_ready, 1)
                    if c == 3 and s.has(n - LV, NB):
                        project_v(s)
                    g = (n - 4) // G
                    if c == 3 and r == 0 and s.has(g, NG):
                        wait(pe, part1_done, s.at(2 * g + 2, 4))
                        misc_free(s, "shift")
                        misc_free(s, "rows")
                        for b in range(G):
                            for t in range(KT):
                                mm = pe.matmul(misc_bank[:, b:b + 1], parts[1][0][:, t, tok(b)], ones_bf[:, 0:1],
                                               start=(t == 0), stop=(t == KT - 1))
                        mm.then_inc(ksum_ready, 1)
                    b, cc = (n - LC, c - 1) if c >= 1 else (n - LC - 1, NC - 1)
                    if s.has(b, NB):
                        weighted_v(s, b, cc)

            run_slots(pe, slot)

        @block.scalar
        def _(act):
            for j, raw in enumerate((proj[0], rest, o_all, recip_all)):
                act.wait_ge(w_in, 64)
                act.activation(w_hi[j][:], raw[:, :, 0:H], ACT.Copy).then_inc(w_hi_done, 1)

            def split_x(g, s):
                wait(act, xT_in, s.at(16 * (g + 1), 32))
                if g > 0:
                    wait(act, qk_ready, s.seqs(G * (g - 1) + 2))
                act.activation(xT_hi[:], xT_raw[:], ACT.Copy).then_inc(x_hi_done, 1)

            def split_c(g, s):
                wait(act, cT_in, s.at(16 * (g + 1), 32))
                if g > 1:
                    wait(act, v_ready, s.seqs(G * (g - 1)))
                    wait(act, qk_ready, s.seqs(G * (g - 1)))
                act.activation(cT_hi[g % 2][:], cT_raw[:], ACT.Copy).then_inc(c_hi_done, 1)

            split_x(0, Slot(0))
            split_c(0, Slot(0))
            act.wait_ge(const_in, 32)
            act.wait_ge(w_lo_done, 4)

            def slot(s):
                n, r = s.n, s.n % G
                for c in range(NC):
                    b = n - LC
                    if s.has(b, NB):
                        if c == 0 and b % G == 0:
                            wait(act, key_bias_done, s.groups(b // G + 1))
                        wait(act, st_ready, s.chunks(NC * b + c + 1))
                        wait(act, pv_ready, s.chunks(NC * (b - 1) + c + 1))
                        act.activation(probs[:, c, :], st_bank[c % 2][:], ACT.Exp,
                                       bias=key_bias[:, b % RING:b % RING + 1], scale=D ** -0.5).then_inc(exp_done, 1)
                    b = n - LC - 1
                    if c == 0 and s.has(b, NB):
                        g = b // G
                        wait(act, pv_ready, s.chunks(NC * (b + 1)))
                        if b % G == 0:
                            wait(act, den_in, s.at(16 * (g - 1), 32))
                            wait(act, num_in, s.at(16 * CH * (g - 1), 32 * CH))
                        act.activation(o_raw[g % 2][:, :, tok(b)], pv_bank[:].rearrange("p (c t) -> p c t", c=NC),
                                       ACT.Copy).then_inc(o_evac, 1)
                    g = (n - 16) // G
                    if c == 0 and r == 0 and s.has(g, NG):
                        wait(act, mult_done, s.at(2 * (g + 1), 4))
                        wait(act, wo_ready, s.seqs(G * g))
                        act.activation(o_hi[:], o_all[:], ACT.Copy).then_inc(o_hi_done, 1)
                    g = n // G + 1
                    if c == 0 and r == 2 and s.has(g, NG):
                        split_c(g, s)
                    b = n - 1 - LV
                    if c == 1 and b % 2 == 1 and s.has(b, NB):
                        wait(act, v_ready, s.seqs(b + 1))
                        wait(act, pv_ready, s.chunks(NC * (b - RING + 1)))
                        act.activation(v_aug[:, (b - 1) % RING:(b - 1) % RING + 2, :, 0:D],
                                       v_bank[:].rearrange("p (b h d) -> p b h d", b=2, d=D),
                                       ACT.Relu).then_inc(v_evac, 1)
                    if c == 2 and s.has(n, NB):
                        g, t, tensor = n // G, r % 2, r // 2
                        wait(act, qk_ready, s.seqs(n + 1))
                        if t == 0:
                            wait(act, part1_done, s.at(2 * (g - 1) + tensor + 1, 4))
                            wait(act, rest_done, s.at(2 * (2 * (g - 1) + tensor + 1), 8))
                        act.activation(proj[tensor][:, t, :], qk_bank[:], ACT.Relu,
                                       bias=bias_qk[:, tensor, t:t + 1]).then_inc(qk_evac, 1)
                    g = n // G + 1
                    if c == 3 and r == 1 and s.has(g, NG):
                        split_x(g, s)
                    g = (n - 21) // G
                    if r == 1 and s.has(g, NG):
                        wait(act, scale_done, s.groups(g + 1))
                        act.activation(z[g % 2][:, c, :], z[g % 2][:, c, :], ACT.Identity,
                                       bias=neg_mean_rstd[:, c:c + 1], scale=rstd[:, c:c + 1]).then_inc(norm_done, 1)

            run_slots(act, slot)

        @block.vector
        def _(dve):
            dve.memset(zeros_bf[:], 0.0)
            dve.wait_ge(bias_in, 16)
            dve.tensor_copy(bias_parts1[:, 0, :], bias_row).then_inc(bias_step, 1)
            dve.wait_ge(bias_step, 1)
            dve.tensor_tensor(bias_rest, bias_row, bias_parts1[:, 0, :], ALU.subtract).then_inc(bias_step, 1)
            dve.wait_ge(bias_step, 2)
            dve.tensor_copy(bias_parts1[:, 1, :], bias_rest).then_inc(bias_step, 1)
            dve.wait_ge(bias_step, 3)
            dve.tensor_tensor(bias_parts1[:, 2, :], bias_rest, bias_parts1[:, 1, :], ALU.subtract).then_inc(bias_step, 1)
            dve.wait_ge(mask_in, 32)
            dve.tensor_copy(masks_bf[:], masks_f).then_inc(masks_done, 1)
            for j, raw in enumerate((proj[0], rest, o_all, recip_all)):
                dve.wait_ge(w_hi_done, j + 1)
                dve.tensor_tensor(w_lo[j][:], raw[:, :, 0:H], w_hi[j][:].bitcast(F32), ALU.subtract).then_inc(w_lo_done, 1)

            def first_part(s, g, tensor):
                wait(dve, qk_evac, s.seqs(G * g + 2 * tensor + 2))
                wait(dve, stack_in[(g - 1) % 2], s.at(16 * STACK_DMAS * ((g - 1) // 2 + 1), 16 * STACK_DMAS))
                if tensor == 1:
                    wait(dve, ksum_ready, s.groups(g))
                dve.tensor_copy(parts[tensor][0][:], proj[tensor][:]).then_inc(part1_done, 1)

            def second_part(s, g, tensor):
                wait(dve, rest_done, s.at(2 * (2 * g + tensor + 1), 8))
                dve.tensor_copy(parts[tensor][1][:], rest[:]).then_inc(part2_done, 1)

            def slot(s):
                n, r = s.n, s.n % G
                for c in range(NC):
                    b = n - LB
                    if s.has(b, NB):
                        wait(dve, s_ready, s.chunks(NC * b + c + 1))
                        if c == 0:
                            wait(dve, parts_done, s.seqs(b - 1))
                        dve.tensor_reduce(neg_max[:, b % 2, CH * c:CH * c + CH],
                                          s_bank[c % 2][:].rearrange("p (h k) -> p h k", k=P),
                                          AX.X, ALU.max, negate=True).then_inc(max_done, 1)
                    if c == NC - 1 and s.has(b, NB):
                        wait(dve, max_done, s.chunks(NC * (b + 1)))
                        wait(dve, shiftT_ready, s.seqs(b - 1))
                        dve.tensor_copy(shift_parts[:, b % 2, 0, :], neg_max[:, b % 2, :]).then_inc(part_a_done, 1)
                        wait(dve, part_a_done, s.seqs(b + 1))
                        dve.tensor_tensor(shift_parts[:, b % 2, 1, :], neg_max[:, b % 2, :], shift_parts[:, b % 2, 0, :],
                                          ALU.subtract).then_inc(parts_done, 1)
                    g = (n - 5) // G
                    if c == 0 and r == 1 and s.has(g, NG):
                        wait(dve, ksum_ready, s.groups(g + 1))
                        wait(dve, exp_done, s.chunks(NC * G * (g - 1)))
                        dve.tensor_scalar(key_bias[:, G * (g % 2):G * (g % 2) + G], misc_bank[:, 0:G], 0.0, -1e30,
                                          ALU.is_equal, ALU.mult).then_inc(key_bias_done, 1)
                    b = n - LB - 1
                    if c == 0 and s.has(b, NB):
                        wait(dve, shiftT_ready, s.seqs(b + 1))
                        wait(dve, shift_in[b % 2], s.at(16 * (b // 2), 16 * RING // 2))
                        dve.tensor_copy(shift[:, b % 2, :], misc_bank[:].bitcast(BF16)[0:2 * NH, 0:P]).then_inc(shift_done, 1)
                    g = (n - 20) // G
                    if c == 0 and r == 0 and s.has(g, NG):
                        wait(dve, aggr_done, s.seqs(G * (g + 1)))
                        wait(dve, std_done, s.groups(g))
                        dve.tensor_scalar(var_n1[:], mean_var[:, g % 2, :, 1], float(H) / (H - 1), None,
                                          ALU.mult).then_inc(var_done, 1)
                    if c == 3 and r == 0 and s.has(g, NG):
                        wait(dve, std_done, s.groups(g + 1))
                        dve.tensor_scalar(std_eps[:], std[:], EPS, None, ALU.add).then_inc(std_eps_done, 1)
                        wait(dve, std_eps_done, s.groups(g + 1))
                        wait(dve, norm_done, s.seqs(G * g))
                        dve.reciprocal(rstd[:], std_eps[:]).then_inc(rstd_done, 1)
                        wait(dve, rstd_done, s.groups(g + 1))
                        dve.scalar_tensor_tensor(neg_mean_rstd[:], mean_var[:, g % 2, :, 0], -1.0, rstd[:],
                                                 ALU.mult, ALU.mult).then_inc(scale_done, 1)
                    g = (n - 14) // G
                    if c == 0 and r == 2 and s.has(g, NG):
                        wait(dve, den_in, s.at(16 * (g + 1), 32))
                        wait(dve, recip_done, s.groups(g))
                        dve.tensor_scalar(den_ok[:], den[:], 1e-30, None, ALU.max).then_inc(den_ok_done, 1)
                        wait(dve, den_ok_done, s.groups(g + 1))
                        wait(dve, recip_out, s.at(16 * g, 32))
                        dve.reciprocal(recip[:], den_ok[:]).then_inc(recip_done, 1)
                    g = (n - 16) // G
                    if c == 1 and r == 0 and s.has(g, NG):
                        wait(dve, o_hi_done, s.groups(g + 1))
                        dve.tensor_tensor(o_lo[:], o_all[:], o_hi[:].bitcast(F32), ALU.subtract).then_inc(o_lo_done, 1)
                    g = (n - 4) // G
                    if c == 2 and r == 0 and s.has(g, NG):
                        second_part(s, g, 1)
                    g = n // G
                    if c == 0 and r == 2 and s.has(g, NG):
                        first_part(s, g, 0)
                    if c == 3 and r == 2 and s.has(g, NG):
                        second_part(s, g, 0)
                    if c == 3 and r == 3 and s.has(g, NG):
                        first_part(s, g, 1)
                    b = n - LW
                    if c == 3 and s.has(b, NB):
                        g = b // G
                        wait(dve, wo_ready, s.seqs(b + 1))
                        if b % G == 0:
                            wait(dve, rows_in[g % 2], s.at(16 * (g // 2 + 1), 16))
                            wait(dve, stored[g % 2], s.at(16 * (g // 2), 16))
                        dve.scalar_tensor_tensor(z[g % 2][:, b % G, :], misc_bank[:, 0:H], 0.0, x_rows[g % 2][:, b % G, :],
                                                 ALU.max, ALU.add).then_inc(z_done, 1)
                        wait(dve, z_done, s.seqs(b + 1))
                        wait(dve, aggr_done, s.seqs(b))
                        dve.bn_stats(stats[:], z[g % 2][:, b % G, :]).then_inc(stats_done, 1)
                        wait(dve, stats_done, s.seqs(b + 1), True)
                        dve.bn_aggr(mean_var[:, g % 2, b % G, :], stats[:]).then_inc(aggr_done, 1)

            run_slots(dve, slot)

        @block.gpsimd
        def _(pool):
            pool.memset(ones_bf[:], 1.0)
            pool.memset(half[:], 0.5)
            pool.memset(id_bf[:], 0.0)
            pool.memset(causal[:], 0.0)
            pool.memset(v_aug[:], 1.0).then_inc(pool_const, 1)
            pool.wait_ge(pool_const, 1)
            pool.affine_select(out=id_bf[:], in_=id_bf[:], compare_op=ALU.not_equal, fill=1.0, base=0,
                               pattern=[[-1, P]], channel_multiplier=1).then_inc(pool_const, 1)
            pool.affine_select(out=causal[:], in_=causal[:], compare_op=ALU.is_ge, fill=-1e30, base=0,
                               pattern=[[1, P]], channel_multiplier=-1).then_inc(pool_const, 1)
            pool.wait_ge(w_lo_done, 4)

            def split_x(g, s):
                wait(pool, x_hi_done, s.groups(g + 1))
                pool.tensor_tensor(xT_lo[:], xT_raw[:], xT_hi[:].bitcast(F32), ALU.subtract).then_inc(x_lo_done, 1)

            def split_c(g, s):
                wait(pool, c_hi_done, s.groups(g + 1))
                pool.tensor_tensor(cT_lo[g % 2][:], cT_raw[:], cT_hi[g % 2][:].bitcast(F32),
                                   ALU.subtract).then_inc(c_lo_done, 1)

            split_x(0, Slot(0))
            split_c(0, Slot(0))

            def rest_of(s, g, tensor):
                wait(pool, part1_done, s.at(2 * g + tensor + 1, 4))
                wait(pool, part3_done, s.at(2 * (2 * g + tensor), 8))
                wait(pool, part2_done, s.at(2 * g + tensor, 4))
                for t in range(KT):
                    pool.tensor_tensor(rest[:, t, :], proj[tensor][:, t, :], parts[tensor][0][:, t, :],
                                       ALU.subtract).then_inc(rest_done, 1)

            def third_of(s, g, tensor):
                wait(pool, part2_done, s.at(2 * g + tensor + 1, 4))
                for t in range(KT):
                    pool.tensor_tensor(parts[tensor][2][:, t, :], rest[:, t, :], parts[tensor][1][:, t, :],
                                       ALU.subtract).then_inc(part3_done, 1)

            def slot(s):
                n, r = s.n, s.n % G
                g = (n - 4) // G
                if r == 0 and s.has(g, NG):
                    rest_of(s, g, 1)
                g = (n - 20) // G
                if r == 0 and s.has(g, NG):
                    wait(pool, var_done, s.groups(g + 1))
                    wait(pool, std_eps_done, s.groups(g))
                    pool.tensor_tensor(std[:], var_n1[:], half[:], ALU.pow).then_inc(std_done, 1)
                g = (n - 4) // G
                if r == 0 and s.has(g, NG):
                    third_of(s, g, 1)
                g = n // G + 1
                if r == 2 and s.has(g, NG):
                    split_x(g, s)
                if r == 2 and s.has(g - 1, NG):
                    rest_of(s, g - 1, 0)
                if r == 2 and s.has(g, NG):
                    split_c(g, s)
                if r == 3 and s.has(g - 1, NG):
                    third_of(s, g - 1, 0)
                g = (n - 15) // G
                if r == 3 and s.has(g, NG):
                    wait(pool, num_in, s.at(16 * CH * (g + 1), 32 * CH))
                    wait(pool, recip_in, s.at(16 * CH * (g + 1), 32 * CH))
                    for t in range(KT):
                        pool.tensor_tensor(o_all[:, t, :], o_all[:, t, :], recip_all[:, t, :], ALU.mult).then_inc(mult_done, 1)

            run_slots(pool, slot)


def kernel(x, ctx_1024, L0_xattn_Wq, L0_xattn_bq, L0_xattn_Wk, L0_xattn_bk, L0_xattn_Wv, L0_xattn_bv,
           L0_xattn_Wo, L0_xattn_bo):
    import concourse.bacc as bacc
    from concourse.bass_utils import run_bass_kernel_spmd

    x, c = np.asarray(x), np.asarray(ctx_1024)
    feature = np.arange(H).reshape(HB, KT, D).transpose(1, 2, 0).reshape(H)
    t, u, d, ch = np.meshgrid(np.arange(KT), np.arange(2), np.arange(D), np.arange(NC), indexing="ij")
    wo_rows = ((CH * ch + 2 * t + u) * D + d).reshape(H)

    q = np.arange(P)
    block = np.arange(MASK_N)[:, None]
    inside = (q // MASK_W == block)
    mask_q = np.where(inside, 2.0 ** (-24 * (q % MASK_W)), 0.0).astype(np.float32)
    mask_k = np.where(inside, -(2.0 ** (24 * (q % MASK_W) + 7)), np.where(q // MASK_W > block, -(2.0 ** 127), 0.0))
    arrays = {
        "xT": np.ascontiguousarray(x.reshape(NB * P, H).T),
        "cT": np.ascontiguousarray(c.reshape(NB * P, H).T),
        "x": np.ascontiguousarray(x),
        "wq": np.ascontiguousarray(np.asarray(L0_xattn_Wq)[:, feature]),
        "wk": np.ascontiguousarray(np.asarray(L0_xattn_Wk)[:, feature]),
        "wv": np.ascontiguousarray(np.asarray(L0_xattn_Wv)),
        "wo": np.ascontiguousarray(np.asarray(L0_xattn_Wo)[wo_rows]),
        "bqk": np.ascontiguousarray(np.stack([np.asarray(b)[feature].reshape(KT, P).T
                                              for b in (L0_xattn_bq, L0_xattn_bk)], axis=1)),
        "bvo": np.ascontiguousarray(np.concatenate([np.asarray(L0_xattn_bv), np.asarray(L0_xattn_bo)])[None, :]),
        "ident": np.eye(P, dtype=np.float32),
        "mask_q": mask_q,
        "mask_k": mask_k.astype(np.float32),
    }
    nc = bacc.Bacc("TRN2", target_bir_lowering=False, num_devices=1,
                   dynamic_dma_scratch_size=1024)
    args = [nc.dram_tensor(name, a.shape, F32, kind="ExternalInput").ap() for name, a in arrays.items()]
    out = nc.dram_tensor("out", (NB, P, H), F32, kind="ExternalOutput").ap()
    build(nc, *args, out)
    r = run_bass_kernel_spmd(nc, [arrays], core_ids=[0])
    return r.results[0]["out"]
```
